# Optimizing a Trainium2 kernel written in Bass

```python
import numpy as np
import jax
import jax.numpy as jnp

def _softmax(x, axis=-1):
    return jax.nn.softmax(x, axis=axis)
def _gelu(x):
    return jax.nn.gelu(x, approximate=True)
def _silu(x):
    return jax.nn.silu(x)
def _sigmoid(x):
    return jax.nn.sigmoid(x)
def _layernorm(x, axis=-1, eps=1e-5):
    m = jnp.mean(x, axis=axis, keepdims=True)
    v = jnp.var(x, axis=axis, keepdims=True)
    return (x - m) / jnp.sqrt(v + eps)
def _scatter_add(tgt, idx, src, axis=0):
    return tgt.at[idx].add(src)
def _segment_sum(src, seg, n):
    return jax.ops.segment_sum(src, seg, n)

kernel_name = 'mk_conv_seq_d4_conv_nhwc96_e15c56'

def setup_inputs(seed: int = 0):
    np.random.seed(seed)
    _w = jnp.asarray
    def _rec_inputs():
        import jax
        import jax.numpy as jnp
        _gk = jax.random.key(seed)
        x = -0.0001372 + 0.9999 * jax.random.normal(jax.random.fold_in(_gk, 1), (8, 224, 224, 96), jnp.float32)
        return x
    x = _rec_inputs()
    def _L0_conv_setup():
        import jax, jax.numpy as jnp
        import numpy as np
        from jax import lax
        BN_EPS = 0.001
        DN = ('NHWC', 'HWIO', 'NHWC')
        key = jax.random.key(seed)
        ks = jax.random.split(key, 8)
        B, H, W, C = (16, 224, 224, 96)
        K = 3
        x = jax.random.normal(ks[0], (B, H, W, C), dtype=jnp.float32)
        dw_kernel = jax.random.normal(ks[1], (K, K, 1, C), dtype=jnp.float32) * 0.1
        dw_bias = jnp.zeros((C,), dtype=jnp.float32)
        pw_kernel = jax.random.normal(ks[2], (1, 1, C, C), dtype=jnp.float32) * 0.1
        pw_bias = jnp.zeros((C,), dtype=jnp.float32)
        gamma = jax.random.uniform(ks[3], (C,), dtype=jnp.float32, minval=0.5, maxval=1.5)
        beta = jax.random.normal(ks[4], (C,), dtype=jnp.float32) * 0.1
        moving_mean = jax.random.normal(ks[5], (C,), dtype=jnp.float32) * 0.1
        moving_var = jax.random.uniform(ks[6], (C,), dtype=jnp.float32, minval=0.5, maxval=1.5)
        return {'x': x, 'dw_kernel': dw_kernel, 'dw_bias': dw_bias, 'pw_kernel': pw_kernel, 'pw_bias': pw_bias, 'gamma': gamma, 'beta': beta, 'moving_mean': moving_mean, 'moving_var': moving_var}
    _L0_conv_all = _L0_conv_setup()
    _L0_conv_in = {k: v for k, v in _L0_conv_all.items() if k in ('dw_kernel', 'dw_bias', 'pw_kernel', 'pw_bias', 'gamma', 'beta', 'moving_mean', 'moving_var', )}
    del _L0_conv_all

    def _L1_conv_setup():
        import jax, jax.numpy as jnp
        import numpy as np
        from jax import lax
        BN_EPS = 0.001
        DN = ('NHWC', 'HWIO', 'NHWC')
        key = jax.random.key(seed)
        ks = jax.random.split(key, 8)
        B, H, W, C = (16, 224, 224, 96)
        K = 3
        x = jax.random.normal(ks[0], (B, H, W, C), dtype=jnp.float32)
        dw_kernel = jax.random.normal(ks[1], (K, K, 1, C), dtype=jnp.float32) * 0.1
        dw_bias = jnp.zeros((C,), dtype=jnp.float32)
        pw_kernel = jax.random.normal(ks[2], (1, 1, C, C), dtype=jnp.float32) * 0.1
        pw_bias = jnp.zeros((C,), dtype=jnp.float32)
        gamma = jax.random.uniform(ks[3], (C,), dtype=jnp.float32, minval=0.5, maxval=1.5)
        beta = jax.random.normal(ks[4], (C,), dtype=jnp.float32) * 0.1
        moving_mean = jax.random.normal(ks[5], (C,), dtype=jnp.float32) * 0.1
        moving_var = jax.random.uniform(ks[6], (C,), dtype=jnp.float32, minval=0.5, maxval=1.5)
        return {'x': x, 'dw_kernel': dw_kernel, 'dw_bias': dw_bias, 'pw_kernel': pw_kernel, 'pw_bias': pw_bias, 'gamma': gamma, 'beta': beta, 'moving_mean': moving_mean, 'moving_var': moving_var}
    _L1_conv_all = _L1_conv_setup()
    _L1_conv_in = {k: v for k, v in _L1_conv_all.items() if k in ('dw_kernel', 'dw_bias', 'pw_kernel', 'pw_bias', 'gamma', 'beta', 'moving_mean', 'moving_var', )}
    del _L1_conv_all

    def _L2_conv_setup():
        import jax, jax.numpy as jnp
        import numpy as np
        from jax import lax
        BN_EPS = 0.001
        DN = ('NHWC', 'HWIO', 'NHWC')
        key = jax.random.key(seed)
        ks = jax.random.split(key, 8)
        B, H, W, C = (16, 224, 224, 96)
        K = 3
        x = jax.random.normal(ks[0], (B, H, W, C), dtype=jnp.float32)
        dw_kernel = jax.random.normal(ks[1], (K, K, 1, C), dtype=jnp.float32) * 0.1
        dw_bias = jnp.zeros((C,), dtype=jnp.float32)
        pw_kernel = jax.random.normal(ks[2], (1, 1, C, C), dtype=jnp.float32) * 0.1
        pw_bias = jnp.zeros((C,), dtype=jnp.float32)
        gamma = jax.random.uniform(ks[3], (C,), dtype=jnp.float32, minval=0.5, maxval=1.5)
        beta = jax.random.normal(ks[4], (C,), dtype=jnp.float32) * 0.1
        moving_mean = jax.random.normal(ks[5], (C,), dtype=jnp.float32) * 0.1
        moving_var = jax.random.uniform(ks[6], (C,), dtype=jnp.float32, minval=0.5, maxval=1.5)
        return {'x': x, 'dw_kernel': dw_kernel, 'dw_bias': dw_bias, 'pw_kernel': pw_kernel, 'pw_bias': pw_bias, 'gamma': gamma, 'beta': beta, 'moving_mean': moving_mean, 'moving_var': moving_var}
    _L2_conv_all = _L2_conv_setup()
    _L2_conv_in = {k: v for k, v in _L2_conv_all.items() if k in ('dw_kernel', 'dw_bias', 'pw_kernel', 'pw_bias', 'gamma', 'beta', 'moving_mean', 'moving_var', )}
    del _L2_conv_all

    def _L3_conv_setup():
        import jax, jax.numpy as jnp
        import numpy as np
        from jax import lax
        BN_EPS = 0.001
        DN = ('NHWC', 'HWIO', 'NHWC')
        key = jax.random.key(seed)
        ks = jax.random.split(key, 8)
        B, H, W, C = (16, 224, 224, 96)
        K = 3
        x = jax.random.normal(ks[0], (B, H, W, C), dtype=jnp.float32)
        dw_kernel = jax.random.normal(ks[1], (K, K, 1, C), dtype=jnp.float32) * 0.1
        dw_bias = jnp.zeros((C,), dtype=jnp.float32)
        pw_kernel = jax.random.normal(ks[2], (1, 1, C, C), dtype=jnp.float32) * 0.1
        pw_bias = jnp.zeros((C,), dtype=jnp.float32)
        gamma = jax.random.uniform(ks[3], (C,), dtype=jnp.float32, minval=0.5, maxval=1.5)
        beta = jax.random.normal(ks[4], (C,), dtype=jnp.float32) * 0.1
        moving_mean = jax.random.normal(ks[5], (C,), dtype=jnp.float32) * 0.1
        moving_var = jax.random.uniform(ks[6], (C,), dtype=jnp.float32, minval=0.5, maxval=1.5)
        return {'x': x, 'dw_kernel': dw_kernel, 'dw_bias': dw_bias, 'pw_kernel': pw_kernel, 'pw_bias': pw_bias, 'gamma': gamma, 'beta': beta, 'moving_mean': moving_mean, 'moving_var': moving_var}
    _L3_conv_all = _L3_conv_setup()
    _L3_conv_in = {k: v for k, v in _L3_conv_all.items() if k in ('dw_kernel', 'dw_bias', 'pw_kernel', 'pw_bias', 'gamma', 'beta', 'moving_mean', 'moving_var', )}
    del _L3_conv_all

    return {
        "x": x,
        "L0_conv_dw_kernel": _L0_conv_in["dw_kernel"],
        "L0_conv_dw_bias": _L0_conv_in["dw_bias"],
        "L0_conv_pw_kernel": _L0_conv_in["pw_kernel"],
        "L0_conv_pw_bias": _L0_conv_in["pw_bias"],
        "L0_conv_gamma": _L0_conv_in["gamma"],
        "L0_conv_beta": _L0_conv_in["beta"],
        "L0_conv_moving_mean": _L0_conv_in["moving_mean"],
        "L0_conv_moving_var": _L0_conv_in["moving_var"],
        "L1_conv_dw_kernel": _L1_conv_in["dw_kernel"],
        "L1_conv_dw_bias": _L1_conv_in["dw_bias"],
        "L1_conv_pw_kernel": _L1_conv_in["pw_kernel"],
        "L1_conv_pw_bias": _L1_conv_in["pw_bias"],
        "L1_conv_gamma": _L1_conv_in["gamma"],
        "L1_conv_beta": _L1_conv_in["beta"],
        "L1_conv_moving_mean": _L1_conv_in["moving_mean"],
        "L1_conv_moving_var": _L1_conv_in["moving_var"],
        "L2_conv_dw_kernel": _L2_conv_in["dw_kernel"],
        "L2_conv_dw_bias": _L2_conv_in["dw_bias"],
        "L2_conv_pw_kernel": _L2_conv_in["pw_kernel"],
        "L2_conv_pw_bias": _L2_conv_in["pw_bias"],
        "L2_conv_gamma": _L2_conv_in["gamma"],
        "L2_conv_beta": _L2_conv_in["beta"],
        "L2_conv_moving_mean": _L2_conv_in["moving_mean"],
        "L2_conv_moving_var": _L2_conv_in["moving_var"],
        "L3_conv_dw_kernel": _L3_conv_in["dw_kernel"],
        "L3_conv_dw_bias": _L3_conv_in["dw_bias"],
        "L3_conv_pw_kernel": _L3_conv_in["pw_kernel"],
        "L3_conv_pw_bias": _L3_conv_in["pw_bias"],
        "L3_conv_gamma": _L3_conv_in["gamma"],
        "L3_conv_beta": _L3_conv_in["beta"],
        "L3_conv_moving_mean": _L3_conv_in["moving_mean"],
        "L3_conv_moving_var": _L3_conv_in["moving_var"],
    }

def reference(x, L0_conv_dw_kernel, L0_conv_dw_bias, L0_conv_pw_kernel, L0_conv_pw_bias, L0_conv_gamma, L0_conv_beta, L0_conv_moving_mean, L0_conv_moving_var, L1_conv_dw_kernel, L1_conv_dw_bias, L1_conv_pw_kernel, L1_conv_pw_bias, L1_conv_gamma, L1_conv_beta, L1_conv_moving_mean, L1_conv_moving_var, L2_conv_dw_kernel, L2_conv_dw_bias, L2_conv_pw_kernel, L2_conv_pw_bias, L2_conv_gamma, L2_conv_beta, L2_conv_moving_mean, L2_conv_moving_var, L3_conv_dw_kernel, L3_conv_dw_bias, L3_conv_pw_kernel, L3_conv_pw_bias, L3_conv_gamma, L3_conv_beta, L3_conv_moving_mean, L3_conv_moving_var):
    import jax
    import jax.numpy as jnp
    def _L0_conv_ref(x, dw_kernel, dw_bias, pw_kernel, pw_bias, gamma, beta, moving_mean, moving_var):
        import jax, jax.numpy as jnp
        import numpy as np
        from jax import lax
        BN_EPS = 0.001
        DN = ('NHWC', 'HWIO', 'NHWC')
        C = x.shape[-1]
        stride = 1
        y = jax.nn.relu(x)
        y = lax.conv_general_dilated(y, dw_kernel, window_strides=(stride, stride), padding='SAME', dimension_numbers=DN, feature_group_count=C)
        y = y + dw_bias
        y = lax.conv_general_dilated(y, pw_kernel, window_strides=(1, 1), padding='SAME', dimension_numbers=DN)
        y = y + pw_bias
        inv = gamma * lax.rsqrt(moving_var + BN_EPS)
        y = y * inv + (beta - moving_mean * inv)
        return y

    def _L1_conv_ref(x, dw_kernel, dw_bias, pw_kernel, pw_bias, gamma, beta, moving_mean, moving_var):
        import jax, jax.numpy as jnp
        import numpy as np
        from jax import lax
        BN_EPS = 0.001
        DN = ('NHWC', 'HWIO', 'NHWC')
        C = x.shape[-1]
        stride = 1
        y = jax.nn.relu(x)
        y = lax.conv_general_dilated(y, dw_kernel, window_strides=(stride, stride), padding='SAME', dimension_numbers=DN, feature_group_count=C)
        y = y + dw_bias
        y = lax.conv_general_dilated(y, pw_kernel, window_strides=(1, 1), padding='SAME', dimension_numbers=DN)
        y = y + pw_bias
        inv = gamma * lax.rsqrt(moving_var + BN_EPS)
        y = y * inv + (beta - moving_mean * inv)
        return y

    def _L2_conv_ref(x, dw_kernel, dw_bias, pw_kernel, pw_bias, gamma, beta, moving_mean, moving_var):
        import jax, jax.numpy as jnp
        import numpy as np
        from jax import lax
        BN_EPS = 0.001
        DN = ('NHWC', 'HWIO', 'NHWC')
        C = x.shape[-1]
        stride = 1
        y = jax.nn.relu(x)
        y = lax.conv_general_dilated(y, dw_kernel, window_strides=(stride, stride), padding='SAME', dimension_numbers=DN, feature_group_count=C)
        y = y + dw_bias
        y = lax.conv_general_dilated(y, pw_kernel, window_strides=(1, 1), padding='SAME', dimension_numbers=DN)
        y = y + pw_bias
        inv = gamma * lax.rsqrt(moving_var + BN_EPS)
        y = y * inv + (beta - moving_mean * inv)
        return y

    def _L3_conv_ref(x, dw_kernel, dw_bias, pw_kernel, pw_bias, gamma, beta, moving_mean, moving_var):
        import jax, jax.numpy as jnp
        import numpy as np
        from jax import lax
        BN_EPS = 0.001
        DN = ('NHWC', 'HWIO', 'NHWC')
        C = x.shape[-1]
        stride = 1
        y = jax.nn.relu(x)
        y = lax.conv_general_dilated(y, dw_kernel, window_strides=(stride, stride), padding='SAME', dimension_numbers=DN, feature_group_count=C)
        y = y + dw_bias
        y = lax.conv_general_dilated(y, pw_kernel, window_strides=(1, 1), padding='SAME', dimension_numbers=DN)
        y = y + pw_bias
        inv = gamma * lax.rsqrt(moving_var + BN_EPS)
        y = y * inv + (beta - moving_mean * inv)
        return y

    def _gn(v, G=32, eps=1e-5):
        B_, H_, W_, C_ = v.shape
        g = v.reshape(B_, H_, W_, G, C_ // G)
        m = jnp.mean(g, axis=(1, 2, 4), keepdims=True)
        s = jnp.var(g, axis=(1, 2, 4), keepdims=True)
        return ((g - m) / jnp.sqrt(s + eps)).reshape(v.shape)

    def _ln_c(v, eps=1e-6):
        m = jnp.mean(v, axis=-1, keepdims=True)
        s = jnp.var(v, axis=-1, keepdims=True)
        return (v - m) / jnp.sqrt(s + eps)

    def _ln_t(v, eps=1e-5):
        m = jnp.mean(v, axis=-1, keepdims=True)
        s = jnp.var(v, axis=-1, keepdims=True)
        return (v - m) / jnp.sqrt(s + eps)

    def _to_tokens(v):
        B_, H_, W_, C_ = v.shape
        return v.reshape(B_, H_ * W_, C_)
    def _from_tokens(t, like):
        return t.reshape(like.shape)

    x = _L0_conv_ref(x, L0_conv_dw_kernel, L0_conv_dw_bias, L0_conv_pw_kernel, L0_conv_pw_bias, L0_conv_gamma, L0_conv_beta, L0_conv_moving_mean, L0_conv_moving_var)
    x = _L1_conv_ref(x, L1_conv_dw_kernel, L1_conv_dw_bias, L1_conv_pw_kernel, L1_conv_pw_bias, L1_conv_gamma, L1_conv_beta, L1_conv_moving_mean, L1_conv_moving_var)
    x = _L2_conv_ref(x, L2_conv_dw_kernel, L2_conv_dw_bias, L2_conv_pw_kernel, L2_conv_pw_bias, L2_conv_gamma, L2_conv_beta, L2_conv_moving_mean, L2_conv_moving_var)
    x = _L3_conv_ref(x, L3_conv_dw_kernel, L3_conv_dw_bias, L3_conv_pw_kernel, L3_conv_pw_bias, L3_conv_gamma, L3_conv_beta, L3_conv_moving_mean, L3_conv_moving_var)
    return x


_drawn_inputs = setup_inputs


def setup_inputs(seed=0):
    import zlib

    import numpy as np

    out = dict(_drawn_inputs(seed))
    spreads = {'L0_conv_dw_bias': (0.0, 0.8),
     'L0_conv_pw_bias': (0.0, 0.8),
     'L1_conv_dw_bias': (0.0, 2.0),
     'L1_conv_pw_bias': (0.0, 2.0),
     'L2_conv_dw_bias': (0.0, 0.8),
     'L2_conv_pw_bias': (0.0, 0.8),
     'L3_conv_dw_bias': (0.0, 0.431),
     'L3_conv_pw_bias': (0.0, 0.466)}
    factors = {'x': 4.633,
     'L0_conv_dw_kernel': 4.278,
     'L0_conv_pw_kernel': 4.173,
     'L0_conv_gamma': 8.0,
     'L0_conv_beta': 33.492,
     'L0_conv_moving_mean': 8.0,
     'L0_conv_moving_var': 8.0,
     'L1_conv_dw_kernel': 3.205,
     'L1_conv_gamma': 5.802,
     'L1_conv_beta': 22.8,
     'L1_conv_moving_mean': 23.585,
     'L1_conv_moving_var': 7.821,
     'L2_conv_beta': 8.0,
     'L2_conv_moving_mean': 8.0,
     'L3_conv_beta': 3.01,
     'L3_conv_moving_mean': 2.931}
    for name, (base, spread) in spreads.items():
        noise = np.random.default_rng([zlib.crc32(name.encode()), seed]).standard_normal(out[name].shape)
        drawn = base * np.exp(spread * noise) if base else spread * noise
        out[name] = jnp.asarray(drawn.astype(out[name].dtype))
    for name, factor in factors.items():
        out[name] = (out[name] * factor).astype(out[name].dtype)
    return out
```

```python
from contextlib import ExitStack

import concourse.bass as bass
from concourse import mybir

F32 = mybir.dt.float32
ALU = mybir.AluOpType
ACT = mybir.ActivationFunctionType

LAYERS = 4
TAPS = 9
LAG = 2
RING_PAIRS = 4
BN_EPS = 0.001
CENTRE = 4
DW_BIAS, PW_BIAS, GAMMA, BETA, MEAN, VAR = range(TAPS, TAPS + 6)
VECTORS = TAPS + 6
VECTOR_NAMES = ["dw_bias", "pw_bias", "gamma", "beta", "moving_mean", "moving_var"]
ORDER = [CENTRE, 0, 1, 2, 3, 5, 6, 7, 8]


def z_taps(u_mod, l):
    return [0, 9, 8, 8][(l - u_mod) % 4]


def conv_stack(nc, x, params, identity_in, out):
    B, H, W, C = x.shape
    ROWS_BLK, ROWS_PAIR = 2, 4
    BLK = ROWS_BLK * W
    PX = 4
    Q = BLK // PX
    RW = W + 2
    RR = 4 * RING_PAIRS + 2
    PAIRS = B * H // ROWS_PAIR
    GROUPS = PAIRS // 4
    IMG = H // 16
    CHUNK = 2
    CBLK = 2 * CHUNK
    OUT_LAG = LAG * (LAYERS - 1) + 1
    LAST_STEP = PAIRS - 1 + OUT_LAG
    assert H % 16 == 0 and BLK <= 512 and BLK % PX == 0 and Q <= 128 and GROUPS % IMG == 0

    x_v = x.rearrange("b h w c -> (b h w c)").rearrange("(n k q f) -> n q k f", k=CBLK, q=Q, f=PX * C)
    out_v = out.rearrange("b h w c -> (b h w c)").rearrange("(n k q f) -> n q k f", k=CBLK, q=Q, f=PX * C)

    ctx = ExitStack()
    with ctx:
        sb = lambda name, shape: ctx.enter_context(nc.sbuf_tensor(name, shape, F32))
        ps = lambda name, shape: ctx.enter_context(nc.psum_tensor(name, shape, F32))
        sem = lambda name: ctx.enter_context(nc.semaphore(name))

        ident = sb("ident", [128, 128])
        vec_rows = sb("vec_rows", [LAYERS * VECTORS, C])
        vec = sb("vec", [C, LAYERS * VECTORS])
        pw = sb("pw", [C, LAYERS, C])
        wt = sb("wt", [C, LAYERS, TAPS, C])
        bn_scale = sb("bn_scale", [C, LAYERS])
        bn_bias = sb("bn_bias", [C, LAYERS])
        tmp = sb("tmp", [C, 8, LAYERS])
        zeros = sb("zeros", [C, W])
        x_in = sb("x_in", [Q, 2, CBLK, PX * C])
        ring = [sb(f"ring{l}", [C, RR * RW]) for l in range(LAYERS)]
        z = sb("z", [C, LAYERS, 2, 2 * BLK])
        y = sb("y", [C, 2, 2 * BLK])
        y_out = sb("y_out", [Q, 2, CBLK, PX * C])

        conv_ps = [ps(f"conv_ps{i}", [C, 2, 512]) for i in range(2)]
        in_ps = [ps(f"in_ps{i}", [C, 512]) for i in range(2)]
        out_ps = [ps(f"out_ps{i}", [Q, 512]) for i in range(2)]

        vectors_loaded = sem("vectors_loaded")
        vectors_transposed = sem("vectors_transposed")
        setup = sem("setup")
        setup_sqrt = sem("setup_sqrt")
        dw_bias_product = sem("dw_bias_product")
        weights_ready = sem("weights_ready")
        rings_cleared = sem("rings_cleared")
        x_loaded = [sem(f"x_loaded{i}") for i in range(2)]
        x_transposed = sem("x_transposed")
        x_in_ring = sem("x_in_ring")
        conv_done = [sem(f"conv_done{l}") for l in range(LAYERS)]
        conv_out = [sem(f"conv_out{l}") for l in range(LAYERS)]
        z_begun = [sem(f"z_begun{l}") for l in range(LAYERS)]
        z_summed = [sem(f"z_summed{l}") for l in range(LAYERS)]
        y_transposed = sem("y_transposed")
        y_ready = sem("y_ready")
        out_stored = [sem(f"out_stored{i}") for i in range(2)]

        ring_rows = [r[:, :].rearrange("c (r w) -> c r w", w=RW) for r in ring]

        def window(l, pos, tap):
            dy, dx = tap // 3, tap % 3
            return ring_rows[l][:, 4 * pos + dy:4 * pos + dy + ROWS_PAIR, dx:dx + W]

        def z_count(u_g, j, l):
            first = j - LAG * l
            n = sum(z_taps((p + LAG * l) % 4, l) > 0 for p in range(first % 4 + 1))
            return 3 * (u_g + first // 4) + n

        def z_sums(g, j, l):
            first = j - LAG * l
            added = [max(z_taps((p + LAG * l) % 4, l) - 1, 0) for p in range(4)]
            return sum(added) * (g + first // 4) + sum(added[:first % 4 + 1])

        def exists(g, p):
            return not isinstance(g, int) or 0 <= 4 * g + p < PAIRS

        def pairs_up_to(g, p):
            return min(4 * g + p + 1, PAIRS) if isinstance(g, int) else 4 * g + (p + 1)

        def positive(n):
            return not isinstance(n, int) or n > 0

        block = ctx.enter_context(nc.Block())

        @block.sync
        def _(sp):
            sp.dma_start(ident[:, :], identity_in).then_inc(vectors_loaded, 16)
            for l in range(LAYERS):
                v0 = l * VECTORS
                sp.dma_start(pw[:, l, :], params[l]["pw_kernel"].rearrange("a b c o -> (a b c) o")).then_inc(vectors_loaded, 16)
                sp.dma_start(vec_rows[v0:v0 + TAPS, :],
                             params[l]["dw_kernel"].rearrange("a b i c -> (a b i) c")).then_inc(vectors_loaded, 16)
                for n, name in enumerate(VECTOR_NAMES):
                    sp.dma_start(vec_rows[v0 + TAPS + n:v0 + TAPS + n + 1, :],
                                 params[l][name].rearrange("(a c) -> a c", a=1)).then_inc(vectors_loaded, 16)

            def load(g, half):
                if not isinstance(g, int) or g > 0:
                    sp.wait_ge(x_transposed, 8 * g + 4 * half - 4)
                sp.dma_start(x_in[:, half, :, :], x_v[2 * g + half, :, :, :] if isinstance(g, int) else
                             x_v[bass.ds(2 * g + half, 1), :, :, :].rearrange("n q k f -> q (n k) f")
                             ).then_inc(x_loaded[half], 16)

            def store(n_half, half):
                sp.wait_ge(y_ready, 8 * n_half + 4 * half + 4)
                sp.dma_start(out_v[2 * n_half + half, :, :, :] if isinstance(n_half, int) else
                             out_v[bass.ds(2 * n_half + half, 1), :, :, :].rearrange("n q k f -> q (n k) f"),
                             y_out[:, half, :, :]).then_inc(out_stored[half], 16)

            for g in range(3):
                for half in range(2):
                    load(g, half)
            with sp.Fori(3, GROUPS) as g:
                load(g, 0)
                store(g - 3, 0)
                load(g, 1)
                store(g - 3, 1)
            for g in range(GROUPS - 3, GROUPS):
                store(g, 0)
                store(g, 1)
            for half in range(2):
                sp.wait_ge(out_stored[half], 16 * GROUPS)

        @block.gpsimd
        def _(pool):
            nc.gpsimd.memset(zeros[:, :], 0.0)
            for r in ring:
                last = nc.gpsimd.memset(r[:, :], 0.0)
            last.then_inc(rings_cleared, 1)

        @block.tensor
        def _(pe):
            pe.wait_ge(vectors_loaded, 16 * (1 + LAYERS * (2 + len(VECTOR_NAMES))))
            nv = LAYERS * VECTORS
            nc.tensor.transpose(in_ps[0][:, 0:nv], vec_rows[:, :], ident[0:nv, 0:nv]).then_inc(vectors_transposed, 1)
            pe.wait_ge(setup, 1)
            for l in range(LAYERS):
                last = nc.tensor.matmul(in_ps[1][:, l:l + 1], pw[:, l, :],
                                        vec[:, l * VECTORS + DW_BIAS:l * VECTORS + DW_BIAS + 1],
                                        start=True, stop=True)
            last.then_inc(dw_bias_product, 1)
            pe.wait_ge(weights_ready, 1)

            def transpose_in(g, j):
                if not exists(g, j):
                    return
                half = j % 4 // CHUNK
                if j % CHUNK == 0:
                    pe.wait_ge(x_loaded[half], 16 * (g + j // 4 + 1))
                for b in range(2):
                    free = 8 * g + 2 * j + b - 1
                    if positive(free):
                        pe.wait_ge(x_in_ring, free)
                    for k in range(PX):
                        last = nc.tensor.transpose(in_ps[b][:, k * Q:(k + 1) * Q],
                                                   x_in[:, half, 2 * (j % CHUNK) + b, k * C:(k + 1) * C],
                                                   ident[0:Q, 0:Q])
                    last.then_inc(x_transposed, 1)

            def transpose_out(g, j):
                if not exists(g, j):
                    return
                pe.wait_ge(conv_out[LAYERS - 1], pairs_up_to(g, j))
                for b in range(2):
                    free = 8 * g + 2 * j + b - 1
                    if positive(free):
                        pe.wait_ge(y_ready, free)
                    pixels = y[:, j % 2, b * BLK:(b + 1) * BLK].rearrange("c (q k) -> c k q", k=PX)
                    for k in range(PX):
                        last = nc.tensor.transpose(out_ps[b][:, k * C:(k + 1) * C], pixels[:, k, :],
                                                   ident[0:C, 0:C])
                    last.then_inc(y_transposed, 1)

            def conv(g, j, l):
                p = j - LAG * l
                if not exists(g, p):
                    return
                if l == 0:
                    pe.wait_ge(x_in_ring, 2 * pairs_up_to(g, p + 1))
                else:
                    pe.wait_ge(conv_out[l - 1], pairs_up_to(g, p + 1))
                turns = [(j - back, k) for back in range(3) for k in (l + 2, l, l - 2)
                         if 0 <= k < LAYERS and (back or k < l) and exists(g, j - back - LAG * k)]
                if turns:
                    step, k = turns[0]
                    pe.wait_ge(conv_out[k], pairs_up_to(g, step - LAG * k))
                taps = z_taps(j % 4, l)
                own = ORDER[taps:]
                for i, tap in enumerate(own):
                    win = window(l, p % 4, tap)
                    for b in range(2):
                        last = nc.tensor.matmul(conv_ps[l % 2][:, b, 0:BLK], wt[:, l, tap, :],
                                                win[:, 2 * b:2 * b + 2, :], start=(i == 0),
                                                stop=(taps == 0 and i == len(own) - 1))
                if taps:
                    pe.wait_ge(z_summed[l], z_sums(g, j, l))
                    for b in range(2):
                        last = nc.tensor.matmul(conv_ps[l % 2][:, b, 0:BLK], pw[:, l, :],
                                                z[:, l, p % 2, b * BLK:(b + 1) * BLK],
                                                start=(len(own) == 0), stop=True)
                last.then_inc(conv_done[l], 1)

            def group(g, steps=4):
                for j in range(steps):
                    transpose_in(g, j + 2)
                    conv(g, j, 0)
                    transpose_out(g, j - OUT_LAG)
                    for l in range(1, LAYERS):
                        conv(g, j, l)

            transpose_in(0, 0)
            transpose_in(0, 1)
            for g in range(2):
                group(g)
            with pe.Fori(2, GROUPS - 1) as g:
                group(g)
            for g in range(GROUPS - 1, LAST_STEP // 4 + 1):
                group(g)

        def z_begin_needs(eng, g, j, l):
            p = j - LAG * l
            if l == 0:
                eng.wait_ge(x_in_ring, 2 * pairs_up_to(g, p + 1))
            else:
                eng.wait_ge(conv_out[l - 1], pairs_up_to(g, p + 1))
            n = pairs_up_to(g, p - 2)
            if positive(n):
                eng.wait_ge(conv_done[l], n)

        def z_pair(l, p):
            return z[:, l, p % 2, :].rearrange("c (r w) -> c r w", w=W)

        @block.scalar
        def _(act):
            act.wait_ge(setup, 2)
            nc.scalar.activation(tmp[:, 1, :], tmp[:, 0, :], ACT.Sqrt).then_inc(setup_sqrt, 1)
            act.wait_ge(rings_cleared, 1)
            act.wait_ge(weights_ready, 1)

            def last_pair(g, p):
                return isinstance(g, int) and 4 * g + p == PAIRS - 1

            def read_in(g, j, gm):
                if not exists(g, j):
                    return
                pos = j % 4
                image_group = None if gm is None else (gm + j // 4) % IMG
                if not isinstance(g, int) or g > 0:
                    act.wait_ge(conv_done[0], 4 * g + j - 2)
                elif 4 * g + j >= RING_PAIRS:
                    act.wait_ge(conv_done[0], 4 * g + j - 2)
                for b in range(2):
                    act.wait_ge(x_transposed, 8 * g + 2 * j + b + 1)
                    rows = in_ps[b][:, 0:BLK].rearrange("c (k r q) -> c r q k", k=PX, r=2)
                    if pos == 0 and b == 0:
                        dup = ring_rows[0][:, RR - 1, 1:W + 1]
                        if image_group == 0:
                            nc.scalar.activation(dup, zeros[:, :], ACT.Copy)
                        else:
                            nc.scalar.activation(dup.rearrange("c (q k) -> c q k", k=PX), rows[:, 0, :, :], ACT.Relu)
                    if last_pair(g, j) and b == 1:
                        nc.scalar.activation(ring_rows[0][:, RR - 1, 1:W + 1], zeros[:, :], ACT.Copy)
                    if pos == 3 and b == 1:
                        dup = ring_rows[0][:, 0, 1:W + 1]
                        if image_group == IMG - 1:
                            nc.scalar.activation(dup, zeros[:, :], ACT.Copy)
                        else:
                            nc.scalar.activation(dup.rearrange("c (q k) -> c q k", k=PX), rows[:, 1, :, :], ACT.Relu)
                    r0 = 1 + 4 * pos + 2 * b
                    nc.scalar.activation(ring_rows[0][:, r0:r0 + 2, 1:W + 1].rearrange("c r (q k) -> c r q k", k=PX),
                                         rows, ACT.Relu).then_inc(x_in_ring, 1)

            def read_conv(g, j, l, gm):
                p = j - LAG * l
                if not exists(g, p):
                    return
                act.wait_ge(conv_done[l], pairs_up_to(g, p))
                src = conv_ps[l % 2]
                scale, bias = bn_scale[:, l:l + 1], bn_bias[:, l:l + 1]
                if l == LAYERS - 1:
                    n = 2 * pairs_up_to(g, p - 2)
                    if positive(n):
                        act.wait_ge(y_transposed, n)
                    nc.scalar.activation(y[:, p % 2, :].rearrange("c (b n) -> c b n", b=2), src[:, :, 0:BLK],
                                         ACT.Identity, bias=bias, scale=scale).then_inc(conv_out[l], 1)
                    return
                n = pairs_up_to(g, p - 3)
                if positive(n):
                    act.wait_ge(conv_done[l + 1], n)
                pos = p % 4
                image_group = None if gm is None else (gm + p // 4) % IMG
                dst = ring_rows[l + 1]
                if pos == 0:
                    if image_group == 0:
                        nc.scalar.activation(dst[:, RR - 1, 1:W + 1], zeros[:, :], ACT.Copy)
                    else:
                        nc.scalar.activation(dst[:, RR - 1, 1:W + 1], src[:, 0, 0:W], ACT.Relu, bias=bias, scale=scale)
                if last_pair(g, p):
                    nc.scalar.activation(dst[:, RR - 1, 1:W + 1], zeros[:, :], ACT.Copy)
                if pos == 3:
                    if image_group == IMG - 1:
                        nc.scalar.activation(dst[:, 0, 1:W + 1], zeros[:, :], ACT.Copy)
                    else:
                        nc.scalar.activation(dst[:, 0, 1:W + 1], src[:, 1, W:BLK], ACT.Relu, bias=bias, scale=scale)
                r0 = 1 + 4 * pos
                nc.scalar.activation(dst[:, r0:r0 + 4, 1:W + 1].rearrange("c (b r) w -> c b r w", b=2),
                                     src[:, :, 0:BLK].rearrange("c b (r w) -> c b r w", w=W),
                                     ACT.Relu, bias=bias, scale=scale).then_inc(conv_out[l], 1)

            def begin_z(g, j, l):
                p = j - LAG * l
                if not exists(g, p) or not z_taps(j % 4, l):
                    return
                z_begin_needs(act, g, j, l)
                tap = l * VECTORS + ORDER[0]
                nc.scalar.activation(z_pair(l, p), window(l, p % 4, ORDER[0]), ACT.Copy,
                                     scale=vec[:, tap:tap + 1]).then_inc(z_begun[l], 1)

            def read_out(g, j):
                if not exists(g, j):
                    return
                half = j % 4 // CHUNK
                if j % CHUNK == 0:
                    n = 16 * (g + j // 4)
                    if positive(n):
                        act.wait_ge(out_stored[half], n)
                for b in range(2):
                    act.wait_ge(y_transposed, 8 * g + 2 * j + b + 1)
                    nc.scalar.activation(y_out[:, half, 2 * (j % CHUNK) + b, :], out_ps[b][:, 0:PX * C],
                                         ACT.Copy).then_inc(y_ready, 1)

            def group(g, gm, first=0):
                for j in range(first, 4):
                    read_in(g, j + 2, gm)
                    begin_z(g, j + 1, 0)
                    read_conv(g, j, 0, gm)
                    begin_z(g, j + 1, 1)
                    read_out(g, j - OUT_LAG)
                    for l in range(1, LAYERS):
                        read_conv(g, j, l, gm)
                        if l + 1 < LAYERS:
                            begin_z(g, j + 1, l + 1)

            read_in(0, 0, 0)
            read_in(0, 1, 0)
            begin_z(0, 0, 0)
            group(0, 0)
            group(1, 1)
            with act.Fori(0, B - 1) as image:
                with act.Fori(2, IMG - 1) as k:
                    group(IMG * image + k, None)
                for k in range(IMG - 1, IMG + 2):
                    group(IMG * image + k, k % IMG)
            with act.Fori(IMG * (B - 1) + 2, GROUPS - 1) as g:
                group(g, None)
            for g in range(GROUPS - 1, LAST_STEP // 4 + 1):
                group(g, g % IMG)

        @block.vector
        def _(dve):
            done = [0]

            def link(instruction):
                done[0] += 1
                instruction.then_inc(setup, 1)
                dve.wait_ge(setup, done[0])

            col = lambda n: vec[:, n:n + VECTORS * (LAYERS - 1) + 1:VECTORS]
            dve.wait_ge(vectors_transposed, 1)
            link(nc.vector.tensor_copy(vec[:, :], in_ps[0][:, 0:LAYERS * VECTORS]))
            link(nc.vector.tensor_scalar_add(tmp[:, 0, :], col(VAR), BN_EPS))
            dve.wait_ge(setup_sqrt, 1)
            link(nc.vector.reciprocal(tmp[:, 2, :], tmp[:, 1, :]))
            link(nc.vector.tensor_tensor(tmp[:, 3, :], tmp[:, 0, :], tmp[:, 2, :], ALU.mult))
            link(nc.vector.tensor_tensor(tmp[:, 4, :], tmp[:, 1, :], tmp[:, 3, :], ALU.add))
            link(nc.vector.tensor_scalar(tmp[:, 5, :], tmp[:, 4, :], 0.5, None, ALU.mult))
            link(nc.vector.reciprocal(tmp[:, 6, :], tmp[:, 5, :]))
            link(nc.vector.tensor_tensor(bn_scale[:, :], col(GAMMA), tmp[:, 6, :], ALU.mult))
            dve.wait_ge(dw_bias_product, 1)
            link(nc.vector.tensor_tensor(tmp[:, 2, :], in_ps[1][:, 0:LAYERS], col(PW_BIAS), ALU.add))
            link(nc.vector.tensor_tensor(tmp[:, 3, :], tmp[:, 2, :], bn_scale[:, :], ALU.mult))
            link(nc.vector.tensor_tensor(tmp[:, 4, :], col(MEAN), bn_scale[:, :], ALU.mult))
            link(nc.vector.tensor_tensor(tmp[:, 5, :], col(BETA), tmp[:, 4, :], ALU.subtract))
            link(nc.vector.tensor_tensor(bn_bias[:, :], tmp[:, 3, :], tmp[:, 5, :], ALU.add))
            for l in range(LAYERS):
                for tap in range(TAPS):
                    n = l * VECTORS + tap
                    last = nc.vector.tensor_scalar(wt[:, l, tap, :], pw[:, l, :], vec[:, n:n + 1], None, ALU.mult)
            last.then_inc(weights_ready, 1)

            def finish_z(g, j, l):
                p = j - LAG * l
                taps = z_taps(j % 4, l)
                if not exists(g, p) or not taps:
                    return
                dve.wait_ge(z_begun[l], z_count(g, j, l))
                acc = z_pair(l, p)
                before = z_sums(g, j, l) - (taps - 1)
                for i, tap in enumerate(ORDER[1:taps]):
                    n = l * VECTORS + tap
                    if i:
                        dve.wait_ge(z_summed[l], before + i)
                    nc.vector.scalar_tensor_tensor(out=acc, in0=window(l, p % 4, tap), scalar=vec[:, n:n + 1],
                                                          in1=acc, op0=ALU.mult, op1=ALU.add
                                                          ).then_inc(z_summed[l], 1)

            def group(g, steps=4):
                for j in range(steps):
                    for l in range(LAYERS):
                        finish_z(g, j + 1, l)

            finish_z(0, 0, 0)
            for g in range(2):
                group(g)
            with dve.Fori(2, GROUPS - 1) as g:
                group(g)
            for g in range(GROUPS - 1, LAST_STEP // 4 + 1):
                group(g)


_PER_LAYER = ["dw_kernel", "pw_kernel"] + VECTOR_NAMES


def kernel(**inputs):
    import numpy as _np
    import concourse.bacc as _bacc
    from concourse import mybir as _mybir
    from concourse.bass_utils import run_bass_kernel_spmd as _run

    nc = _bacc.Bacc("TRN2", target_bir_lowering=False, num_devices=1)
    arrays = {}

    def given(name, a):
        arrays[name] = a = _np.ascontiguousarray(a)
        return nc.dram_tensor(name, a.shape, _mybir.dt.from_np(a.dtype), kind="ExternalInput").ap()

    x = given("in_x_dram", inputs["x"])
    params = [{n: given(f"in_L{l}_{n}_dram", inputs[f"L{l}_conv_{n}"]) for n in _PER_LAYER} for l in range(LAYERS)]
    identity = given("in_identity_dram", _np.eye(128, dtype=_np.float32))
    out = nc.dram_tensor("out_0_dram", inputs["x"].shape, _mybir.dt.float32, kind="ExternalOutput").ap()
    conv_stack(nc, x, params, identity, out)
    r = _run(nc, [arrays], core_ids=[0])
    return r.results[0]["out_0_dram"]
```

```python
from contextlib import ExitStack

import concourse.bass as bass
from concourse import mybir

F32 = mybir.dt.float32
ALU = mybir.AluOpType
ACT = mybir.ActivationFunctionType

LAYERS = 4
TAPS = 9
LAG = 2
RING_PAIRS = 4
BN_EPS = 0.001
DW_BIAS, PW_BIAS, GAMMA, BETA, MEAN, VAR = range(TAPS, TAPS + 6)
VECTORS = TAPS + 6
VECTOR_NAMES = ["dw_bias", "pw_bias", "gamma", "beta", "moving_mean", "moving_var"]


DMA_TAPS = [2, 2, 2, 2]
DVE_TAPS = [4, 4, 4, 5]


def dma_taps(u_mod, l):
    return DMA_TAPS[(l - u_mod) % 4]


def dve_taps(u_mod, l):
    return DVE_TAPS[(l - u_mod) % 4]


def z_taps(u_mod, l):
    return 1 + dma_taps(u_mod, l) + dve_taps(u_mod, l)


def conv_stack(nc, x, params, identity_in, out):
    B, H, W, C = x.shape
    ROWS_BLK, ROWS_PAIR = 2, 4
    BLK = ROWS_BLK * W
    PX = 4
    Q = BLK // PX
    RW = W + 2
    RR = 4 * RING_PAIRS + 2
    PAIRS = B * H // ROWS_PAIR
    GROUPS = PAIRS // 4
    IMG = H // 16
    CHUNK = 2
    CBLK = 2 * CHUNK
    OUT_LAG = LAG * (LAYERS - 1) + 1
    LAST_STEP = PAIRS - 1 + OUT_LAG
    assert H % 16 == 0 and BLK <= 512 and BLK % PX == 0 and Q <= 128 and GROUPS % IMG == 0

    x_v = x.rearrange("b h w c -> (b h w c)").rearrange("(n k q f) -> n q k f", k=CBLK, q=Q, f=PX * C)
    out_v = out.rearrange("b h w c -> (b h w c)").rearrange("(n k q f) -> n q k f", k=CBLK, q=Q, f=PX * C)

    ctx = ExitStack()
    with ctx:
        sb = lambda name, shape: ctx.enter_context(nc.sbuf_tensor(name, shape, F32))
        ps = lambda name, shape: ctx.enter_context(nc.psum_tensor(name, shape, F32))
        sem = lambda name: ctx.enter_context(nc.semaphore(name))

        ident = sb("ident", [128, 128])
        vec_rows = sb("vec_rows", [LAYERS * VECTORS, C])
        vec = sb("vec", [C, LAYERS * VECTORS])
        pw = sb("pw", [C, LAYERS, C])
        wt = sb("wt", [C, LAYERS, TAPS, C])
        bn_scale = sb("bn_scale", [C, LAYERS])
        bn_bias = sb("bn_bias", [C, LAYERS])
        tmp = sb("tmp", [C, 8, LAYERS])
        zeros = sb("zeros", [C, W])
        x_in = sb("x_in", [Q, 2, CBLK, PX * C])
        ring = [sb(f"ring{l}", [C, RR * RW]) for l in range(LAYERS)]
        z = sb("z", [C, LAYERS, 2, 2 * BLK])
        products = sb("products", [C, LAYERS, max(DMA_TAPS), 2 * BLK])
        y = sb("y", [C, 2, 2 * BLK])
        y_out = sb("y_out", [Q, 2, CBLK, PX * C])

        conv_ps = [ps(f"conv_ps{i}", [C, 2, 512]) for i in range(2)]
        in_ps = [ps(f"in_ps{i}", [C, 512]) for i in range(2)]
        out_ps = [ps(f"out_ps{i}", [Q, 512]) for i in range(2)]

        vectors_loaded = sem("vectors_loaded")
        vectors_transposed = sem("vectors_transposed")
        setup = sem("setup")
        setup_sqrt = sem("setup_sqrt")
        dw_bias_product = sem("dw_bias_product")
        weights_ready = sem("weights_ready")
        rings_cleared = sem("rings_cleared")
        x_loaded = [sem(f"x_loaded{i}") for i in range(2)]
        x_transposed = sem("x_transposed")
        x_in_ring = sem("x_in_ring")
        conv_done = [sem(f"conv_done{l}") for l in range(LAYERS)]
        conv_out = [sem(f"conv_out{l}") for l in range(LAYERS)]
        z_begun = [sem(f"z_begun{l}") for l in range(LAYERS)]
        z_summed = [sem(f"z_summed{l}") for l in range(LAYERS)]
        products_ready = [sem(f"products_ready{l}") for l in range(LAYERS)]
        products_summed = [sem(f"products_summed{l}") for l in range(LAYERS)]
        z_complete = [sem(f"z_complete{l}") for l in range(LAYERS)]
        adds_begun = sem("adds_begun")
        y_transposed = sem("y_transposed")
        y_ready = sem("y_ready")
        out_stored = [sem(f"out_stored{i}") for i in range(2)]

        ring_rows = [r[:, :].rearrange("c (r w) -> c r w", w=RW) for r in ring]

        def window(l, pos, tap):
            dy, dx = tap // 3, tap % 3
            return ring_rows[l][:, 4 * pos + dy:4 * pos + dy + ROWS_PAIR, dx:dx + W]

        def count(g, j, l, of):
            first = j - LAG * l
            each = [of((p + LAG * l) % 4, l) for p in range(4)]
            return sum(each) * (g + first // 4) + sum(each[:first % 4 + 1])

        def z_sums(g, j, l):
            return count(g, j, l, dve_taps)

        def product_sums(g, j, l):
            return count(g, j, l, lambda u, l: max(dma_taps(u, l) - 1, 0))

        def exists(g, p):
            return not isinstance(g, int) or 0 <= 4 * g + p < PAIRS

        def pairs_up_to(g, p):
            return min(4 * g + p + 1, PAIRS) if isinstance(g, int) else 4 * g + (p + 1)

        def positive(n):
            return not isinstance(n, int) or n > 0

        block = ctx.enter_context(nc.Block())

        @block.sync
        def _(sp):
            sp.dma_start(ident[:, :], identity_in).then_inc(vectors_loaded, 16)
            for l in range(LAYERS):
                v0 = l * VECTORS
                sp.dma_start(pw[:, l, :], params[l]["pw_kernel"].rearrange("a b c o -> (a b c) o")).then_inc(vectors_loaded, 16)
                sp.dma_start(vec_rows[v0:v0 + TAPS, :],
                             params[l]["dw_kernel"].rearrange("a b i c -> (a b i) c")).then_inc(vectors_loaded, 16)
                for n, name in enumerate(VECTOR_NAMES):
                    sp.dma_start(vec_rows[v0 + TAPS + n:v0 + TAPS + n + 1, :],
                                 params[l][name].rearrange("(a c) -> a c", a=1)).then_inc(vectors_loaded, 16)

            def load(g, half):
                if not isinstance(g, int) or g > 0:
                    sp.wait_ge(x_transposed, 8 * g + 4 * half - 4)
                sp.dma_start(x_in[:, half, :, :], x_v[2 * g + half, :, :, :] if isinstance(g, int) else
                             x_v[bass.ds(2 * g + half, 1), :, :, :].rearrange("n q k f -> q (n k) f")
                             ).then_inc(x_loaded[half], 16)

            def store(n_half, half):
                sp.wait_ge(y_ready, 8 * n_half + 4 * half + 4)
                sp.dma_start(out_v[2 * n_half + half, :, :, :] if isinstance(n_half, int) else
                             out_v[bass.ds(2 * n_half + half, 1), :, :, :].rearrange("n q k f -> q (n k) f"),
                             y_out[:, half, :, :]).then_inc(out_stored[half], 16)

            for g in range(3):
                for half in range(2):
                    load(g, half)
            with sp.Fori(3, GROUPS) as g:
                load(g, 0)
                store(g - 3, 0)
                load(g, 1)
                store(g - 3, 1)
            for g in range(GROUPS - 3, GROUPS):
                store(g, 0)
                store(g, 1)
            for half in range(2):
                sp.wait_ge(out_stored[half], 16 * GROUPS)

        @block.gpsimd
        def _(pool):
            nc.gpsimd.memset(zeros[:, :], 0.0)
            for r in ring:
                last = nc.gpsimd.memset(r[:, :], 0.0)
            last.then_inc(rings_cleared, 1)

            def add(into, addend):
                pool.sem_inc(adds_begun, 1)
                return pool.dma_start(into, addend, accum_op=ALU.add)

            def sum_products(g, j, l):
                if not exists(g, j - LAG * l):
                    return
                pool.wait_ge(products_ready[l], pairs_up_to(g, j - LAG * l))
                n = dma_taps(j % 4, l) - 1
                for k in range(n):
                    if k:
                        pool.wait_ge(products_summed[l], 16 * (product_sums(g, j, l) - n + k))
                    add(products[:, l, 0, :], products[:, l, 1 + k, :]).then_inc(products_summed[l], 16)

            def complete_z(g, j, l):
                p = j - LAG * l
                if not exists(g, p):
                    return
                pool.wait_ge(z_summed[l], z_sums(g, j, l))
                n = product_sums(g, j, l)
                if positive(n):
                    pool.wait_ge(products_summed[l], 16 * n)
                add(z[:, l, p % 2, :], products[:, l, 0, :]).then_inc(z_complete[l], 16)

            def group(g):
                for j in range(4):
                    for l in range(LAYERS):
                        sum_products(g, j + 1, l)
                        complete_z(g, j + 1 if l else j, (l - 1) % LAYERS)

            sum_products(0, 0, 0)
            complete_z(0, 0, 0)
            for g in range(2):
                group(g)
            with pool.Fori(2, GROUPS - 1) as g:
                group(g)
            for g in range(GROUPS - 1, LAST_STEP // 4 + 1):
                group(g)

        @block.tensor
        def _(pe):
            pe.wait_ge(vectors_loaded, 16 * (1 + LAYERS * (2 + len(VECTOR_NAMES))))
            nv = LAYERS * VECTORS
            nc.tensor.transpose(in_ps[0][:, 0:nv], vec_rows[:, :], ident[0:nv, 0:nv]).then_inc(vectors_transposed, 1)
            pe.wait_ge(setup, 1)
            for l in range(LAYERS):
                last = nc.tensor.matmul(in_ps[1][:, l:l + 1], pw[:, l, :],
                                        vec[:, l * VECTORS + DW_BIAS:l * VECTORS + DW_BIAS + 1],
                                        start=True, stop=True)
            last.then_inc(dw_bias_product, 1)
            pe.wait_ge(weights_ready, 1)

            def transpose_in(g, j):
                if not exists(g, j):
                    return
                half = j % 4 // CHUNK
                if j % CHUNK == 0:
                    pe.wait_ge(x_loaded[half], 16 * (g + j // 4 + 1))
                for b in range(2):
                    free = 8 * g + 2 * j + b - 1
                    if positive(free):
                        pe.wait_ge(x_in_ring, free)
                    for k in range(PX):
                        last = nc.tensor.transpose(in_ps[b][:, k * Q:(k + 1) * Q],
                                                   x_in[:, half, 2 * (j % CHUNK) + b, k * C:(k + 1) * C],
                                                   ident[0:Q, 0:Q])
                    last.then_inc(x_transposed, 1)

            def transpose_out(g, j):
                if not exists(g, j):
                    return
                pe.wait_ge(conv_out[LAYERS - 1], pairs_up_to(g, j))
                for b in range(2):
                    free = 8 * g + 2 * j + b - 1
                    if positive(free):
                        pe.wait_ge(y_ready, free)
                    pixels = y[:, j % 2, b * BLK:(b + 1) * BLK].rearrange("c (q k) -> c k q", k=PX)
                    for k in range(PX):
                        last = nc.tensor.transpose(out_ps[b][:, k * C:(k + 1) * C], pixels[:, k, :],
                                                   ident[0:C, 0:C])
                    last.then_inc(y_transposed, 1)

            def conv(g, j, l):
                p = j - LAG * l
                if not exists(g, p):
                    return
                if l == 0:
                    pe.wait_ge(x_in_ring, 2 * pairs_up_to(g, p + 1))
                else:
                    pe.wait_ge(conv_out[l - 1], pairs_up_to(g, p + 1))
                turns = [(j - back, k) for back in range(3) for k in (l + 2, l, l - 2)
                         if 0 <= k < LAYERS and (back or k < l) and exists(g, j - back - LAG * k)]
                if turns:
                    step, k = turns[0]
                    pe.wait_ge(conv_out[k], pairs_up_to(g, step - LAG * k))
                taps = z_taps(j % 4, l)
                own = range(taps, TAPS)
                for i, tap in enumerate(own):
                    win = window(l, p % 4, tap)
                    for b in range(2):
                        last = nc.tensor.matmul(conv_ps[l % 2][:, b, 0:BLK], wt[:, l, tap, :],
                                                win[:, 2 * b:2 * b + 2, :], start=(i == 0), stop=False)
                pe.wait_ge(z_complete[l], 16 * pairs_up_to(g, p))
                for b in range(2):
                    last = nc.tensor.matmul(conv_ps[l % 2][:, b, 0:BLK], pw[:, l, :],
                                            z[:, l, p % 2, b * BLK:(b + 1) * BLK],
                                            start=(len(own) == 0), stop=True)
                last.then_inc(conv_done[l], 1)

            def group(g, steps=4):
                for j in range(steps):
                    transpose_in(g, j + 2)
                    conv(g, j, 0)
                    transpose_out(g, j - OUT_LAG)
                    for l in range(1, LAYERS):
                        conv(g, j, l)

            transpose_in(0, 0)
            transpose_in(0, 1)
            for g in range(2):
                group(g)
            with pe.Fori(2, GROUPS - 1) as g:
                group(g)
            for g in range(GROUPS - 1, LAST_STEP // 4 + 1):
                group(g)

        def inputs_in_ring(eng, g, j, l):
            p = j - LAG * l
            if l == 0:
                eng.wait_ge(x_in_ring, 2 * pairs_up_to(g, p + 1))
            else:
                eng.wait_ge(conv_out[l - 1], pairs_up_to(g, p + 1))

        def z_pair(l, p):
            return z[:, l, p % 2, :].rearrange("c (r w) -> c r w", w=W)

        @block.scalar
        def _(act):
            act.wait_ge(setup, 2)
            nc.scalar.activation(tmp[:, 1, :], tmp[:, 0, :], ACT.Sqrt).then_inc(setup_sqrt, 1)
            act.wait_ge(rings_cleared, 1)
            act.wait_ge(weights_ready, 1)

            def last_pair(g, p):
                return isinstance(g, int) and 4 * g + p == PAIRS - 1

            def read_in(g, j, gm):
                if not exists(g, j):
                    return
                pos = j % 4
                image_group = None if gm is None else (gm + j // 4) % IMG
                if not isinstance(g, int) or g > 0:
                    act.wait_ge(conv_done[0], 4 * g + j - 2)
                elif 4 * g + j >= RING_PAIRS:
                    act.wait_ge(conv_done[0], 4 * g + j - 2)
                for b in range(2):
                    act.wait_ge(x_transposed, 8 * g + 2 * j + b + 1)
                    rows = in_ps[b][:, 0:BLK].rearrange("c (k r q) -> c r q k", k=PX, r=2)
                    if pos == 0 and b == 0:
                        dup = ring_rows[0][:, RR - 1, 1:W + 1]
                        if image_group == 0:
                            nc.scalar.activation(dup, zeros[:, :], ACT.Copy)
                        else:
                            nc.scalar.activation(dup.rearrange("c (q k) -> c q k", k=PX), rows[:, 0, :, :], ACT.Relu)
                    if last_pair(g, j) and b == 1:
                        nc.scalar.activation(ring_rows[0][:, RR - 1, 1:W + 1], zeros[:, :], ACT.Copy)
                    if pos == 3 and b == 1:
                        dup = ring_rows[0][:, 0, 1:W + 1]
                        if image_group == IMG - 1:
                            nc.scalar.activation(dup, zeros[:, :], ACT.Copy)
                        else:
                            nc.scalar.activation(dup.rearrange("c (q k) -> c q k", k=PX), rows[:, 1, :, :], ACT.Relu)
                    r0 = 1 + 4 * pos + 2 * b
                    nc.scalar.activation(ring_rows[0][:, r0:r0 + 2, 1:W + 1].rearrange("c r (q k) -> c r q k", k=PX),
                                         rows, ACT.Relu).then_inc(x_in_ring, 1)

            def read_conv(g, j, l, gm):
                p = j - LAG * l
                if not exists(g, p):
                    return
                act.wait_ge(conv_done[l], pairs_up_to(g, p))
                src = conv_ps[l % 2]
                scale, bias = bn_scale[:, l:l + 1], bn_bias[:, l:l + 1]
                if l == LAYERS - 1:
                    n = 2 * pairs_up_to(g, p - 2)
                    if positive(n):
                        act.wait_ge(y_transposed, n)
                    nc.scalar.activation(y[:, p % 2, :].rearrange("c (b n) -> c b n", b=2), src[:, :, 0:BLK],
                                         ACT.Identity, bias=bias, scale=scale).then_inc(conv_out[l], 1)
                    return
                n = pairs_up_to(g, p - 3)
                if positive(n):
                    act.wait_ge(conv_done[l + 1], n)
                pos = p % 4
                image_group = None if gm is None else (gm + p // 4) % IMG
                dst = ring_rows[l + 1]
                if pos == 0:
                    if image_group == 0:
                        nc.scalar.activation(dst[:, RR - 1, 1:W + 1], zeros[:, :], ACT.Copy)
                    else:
                        nc.scalar.activation(dst[:, RR - 1, 1:W + 1], src[:, 0, 0:W], ACT.Relu, bias=bias, scale=scale)
                if last_pair(g, p):
                    nc.scalar.activation(dst[:, RR - 1, 1:W + 1], zeros[:, :], ACT.Copy)
                if pos == 3:
                    if image_group == IMG - 1:
                        nc.scalar.activation(dst[:, 0, 1:W + 1], zeros[:, :], ACT.Copy)
                    else:
                        nc.scalar.activation(dst[:, 0, 1:W + 1], src[:, 1, W:BLK], ACT.Relu, bias=bias, scale=scale)
                r0 = 1 + 4 * pos
                nc.scalar.activation(dst[:, r0:r0 + 4, 1:W + 1].rearrange("c (b r) w -> c b r w", b=2),
                                     src[:, :, 0:BLK].rearrange("c b (r w) -> c b r w", w=W),
                                     ACT.Relu, bias=bias, scale=scale).then_inc(conv_out[l], 1)

            def begin_z(g, j, l):
                p = j - LAG * l
                if not exists(g, p):
                    return
                inputs_in_ring(act, g, j, l)
                n = pairs_up_to(g, p - 2)
                if positive(n):
                    act.wait_ge(conv_done[l], n)
                nc.scalar.activation(z_pair(l, p), window(l, p % 4, 0), ACT.Copy,
                                     scale=vec[:, l * VECTORS:l * VECTORS + 1]).then_inc(z_begun[l], 1)
                before = pairs_up_to(g, p - 1)
                if positive(before):
                    act.wait_ge(z_complete[l], 16 * before)
                for k in range(dma_taps(j % 4, l)):
                    tap = l * VECTORS + 1 + k
                    last = nc.scalar.activation(products[:, l, k, :].rearrange("c (r w) -> c r w", w=W),
                                                window(l, p % 4, 1 + k), ACT.Copy, scale=vec[:, tap:tap + 1])
                last.then_inc(products_ready[l], 1)

            def read_out(g, j):
                if not exists(g, j):
                    return
                half = j % 4 // CHUNK
                if j % CHUNK == 0:
                    n = 16 * (g + j // 4)
                    if positive(n):
                        act.wait_ge(out_stored[half], n)
                for b in range(2):
                    act.wait_ge(y_transposed, 8 * g + 2 * j + b + 1)
                    nc.scalar.activation(y_out[:, half, 2 * (j % CHUNK) + b, :], out_ps[b][:, 0:PX * C],
                                         ACT.Copy).then_inc(y_ready, 1)

            def group(g, gm, first=0):
                for j in range(first, 4):
                    read_in(g, j + 2, gm)
                    begin_z(g, j + 1, 0)
                    read_conv(g, j, 0, gm)
                    begin_z(g, j + 1, 1)
                    read_out(g, j - OUT_LAG)
                    for l in range(1, LAYERS):
                        read_conv(g, j, l, gm)
                        if l + 1 < LAYERS:
                            begin_z(g, j + 1, l + 1)

            read_in(0, 0, 0)
            read_in(0, 1, 0)
            begin_z(0, 0, 0)
            group(0, 0)
            group(1, 1)
            with act.Fori(0, B - 1) as image:
                with act.Fori(2, IMG - 1) as k:
                    group(IMG * image + k, None)
                for k in range(IMG - 1, IMG + 2):
                    group(IMG * image + k, k % IMG)
            with act.Fori(IMG * (B - 1) + 2, GROUPS - 1) as g:
                group(g, None)
            for g in range(GROUPS - 1, LAST_STEP // 4 + 1):
                group(g, g % IMG)

        @block.vector
        def _(dve):
            done = [0]

            def link(instruction):
                done[0] += 1
                instruction.then_inc(setup, 1)
                dve.wait_ge(setup, done[0])

            col = lambda n: vec[:, n:n + VECTORS * (LAYERS - 1) + 1:VECTORS]
            dve.wait_ge(vectors_transposed, 1)
            link(nc.vector.tensor_copy(vec[:, :], in_ps[0][:, 0:LAYERS * VECTORS]))
            link(nc.vector.tensor_scalar_add(tmp[:, 0, :], col(VAR), BN_EPS))
            dve.wait_ge(setup_sqrt, 1)
            link(nc.vector.reciprocal(tmp[:, 2, :], tmp[:, 1, :]))
            link(nc.vector.tensor_tensor(tmp[:, 3, :], tmp[:, 0, :], tmp[:, 2, :], ALU.mult))
            link(nc.vector.tensor_tensor(tmp[:, 4, :], tmp[:, 1, :], tmp[:, 3, :], ALU.add))
            link(nc.vector.tensor_scalar(tmp[:, 5, :], tmp[:, 4, :], 0.5, None, ALU.mult))
            link(nc.vector.reciprocal(tmp[:, 6, :], tmp[:, 5, :]))
            link(nc.vector.tensor_tensor(bn_scale[:, :], col(GAMMA), tmp[:, 6, :], ALU.mult))
            dve.wait_ge(dw_bias_product, 1)
            link(nc.vector.tensor_tensor(tmp[:, 2, :], in_ps[1][:, 0:LAYERS], col(PW_BIAS), ALU.add))
            link(nc.vector.tensor_tensor(tmp[:, 3, :], tmp[:, 2, :], bn_scale[:, :], ALU.mult))
            link(nc.vector.tensor_tensor(tmp[:, 4, :], col(MEAN), bn_scale[:, :], ALU.mult))
            link(nc.vector.tensor_tensor(tmp[:, 5, :], col(BETA), tmp[:, 4, :], ALU.subtract))
            link(nc.vector.tensor_tensor(bn_bias[:, :], tmp[:, 3, :], tmp[:, 5, :], ALU.add))
            for l in range(LAYERS):
                for tap in range(TAPS):
                    n = l * VECTORS + tap
                    last = nc.vector.tensor_scalar(wt[:, l, tap, :], pw[:, l, :], vec[:, n:n + 1], None, ALU.mult)
            last.then_inc(weights_ready, 1)

            def sum_taps(g, j, l, late):
                p = j - LAG * l
                if not exists(g, p):
                    return
                taps = range(1 + dma_taps(j % 4, l), z_taps(j % 4, l))
                before = z_sums(g, j, l) - len(taps)
                acc = z_pair(l, p)
                half = len(taps) // 2
                if not late:
                    dve.wait_ge(z_begun[l], pairs_up_to(g, p))
                for i in range(half, len(taps)) if late else range(half):
                    tap = taps[i]
                    weight = vec[:, l * VECTORS + tap:l * VECTORS + tap + 1]
                    if i:
                        dve.wait_ge(z_summed[l], before + i)
                    nc.vector.scalar_tensor_tensor(out=acc, in0=window(l, p % 4, tap), scalar=weight, in1=acc,
                                                   op0=ALU.mult, op1=ALU.add).then_inc(z_summed[l], 1)
                    yield

            def sum_z(g, j, l):
                turns = [sum_taps(g, j if l else j - 1, (l - 1) % LAYERS, True), sum_taps(g, j, l, False)]
                while turns:
                    turns = [t for t in turns if next(t, turns) is not turns]

            def group(g, steps=4):
                for j in range(steps):
                    for l in range(LAYERS):
                        sum_z(g, j + 1, l)

            for l in range(LAYERS):
                sum_z(0, 0, l)
            for g in range(2):
                group(g)
            with dve.Fori(2, GROUPS - 1) as g:
                group(g)
            for g in range(GROUPS - 1, LAST_STEP // 4 + 1):
                group(g)


_PER_LAYER = ["dw_kernel", "pw_kernel"] + VECTOR_NAMES


def kernel(**inputs):
    import numpy as _np
    import concourse.bacc as _bacc
    from concourse import mybir as _mybir
    from concourse.bass_utils import run_bass_kernel_spmd as _run

    nc = _bacc.Bacc("TRN2", target_bir_lowering=False, num_devices=1)
    arrays = {}

    def given(name, a):
        arrays[name] = a = _np.ascontiguousarray(a)
        return nc.dram_tensor(name, a.shape, _mybir.dt.from_np(a.dtype), kind="ExternalInput").ap()

    x = given("in_x_dram", inputs["x"])
    params = [{n: given(f"in_L{l}_{n}_dram", inputs[f"L{l}_conv_{n}"]) for n in _PER_LAYER} for l in range(LAYERS)]
    identity = given("in_identity_dram", _np.eye(128, dtype=_np.float32))
    out = nc.dram_tensor("out_0_dram", inputs["x"].shape, _mybir.dt.float32, kind="ExternalOutput").ap()
    conv_stack(nc, x, params, identity, out)
    r = _run(nc, [arrays], core_ids=[0])
    return r.results[0]["out_0_dram"]
```

```python
from contextlib import ExitStack

import concourse.bass as bass
from concourse import mybir

F32 = mybir.dt.float32
F32R = mybir.dt.float32r
ALU = mybir.AluOpType
ACT = mybir.ActivationFunctionType

LAYERS = 4
SPLIT = LAYERS - 1
TAPS = 9
X_LEAD = 3
LAG = 2
RING_PAIRS = 4
BN_EPS = 0.001
DW_BIAS, PW_BIAS, GAMMA, BETA, MEAN, VAR = range(TAPS, TAPS + 6)
VECTORS = TAPS + 6
VECTOR_NAMES = ["dw_bias", "pw_bias", "gamma", "beta", "moving_mean", "moving_var"]


DMA_TAPS = [[2, 3, 3], [2, 3, 3], [2, 3, 3], [2, 3, 3]]
DVE_TAPS = [[5, 5, 5], [5, 5, 5], [6, 5, 5], [5, 5, 5]]


def dma_taps(u_mod, l):
    return DMA_TAPS[u_mod][l]


def dve_taps(u_mod, l):
    return DVE_TAPS[u_mod][l]


def z_taps(u_mod, l):
    return 1 + dma_taps(u_mod, l) + dve_taps(u_mod, l)


def conv_stack(nc, x, params, identity_in, out):
    B, H, W, C = x.shape
    ROWS_BLK, ROWS_PAIR = 2, 4
    BLK = ROWS_BLK * W
    PX = 4
    Q = BLK // PX
    RW = W + 2
    RR = 4 * RING_PAIRS + 2
    PAIRS = B * H // ROWS_PAIR
    GROUPS = PAIRS // 4
    IMG = H // 16
    CHUNK = 2
    CBLK = 2 * CHUNK
    OUT_LAG = LAG * (LAYERS - 1) + 1
    LAST_STEP = PAIRS - 1 + OUT_LAG
    PEELED = 3
    assert H % 16 == 0 and BLK <= 512 and BLK % PX == 0 and Q <= 128 and GROUPS % IMG == 0

    x_v = x.rearrange("b h w c -> (b h w c)").rearrange("(n k q f) -> n q k f", k=CBLK, q=Q, f=PX * C)
    out_v = out.rearrange("b h w c -> (b h w c)").rearrange("(n k q f) -> n q k f", k=CBLK, q=Q, f=PX * C)

    ctx = ExitStack()
    with ctx:
        sb = lambda name, shape, dtype=F32: ctx.enter_context(nc.sbuf_tensor(name, shape, dtype))
        ps = lambda name, shape: ctx.enter_context(nc.psum_tensor(name, shape, F32))
        sem = lambda name: ctx.enter_context(nc.semaphore(name))

        ident = sb("ident", [128, 128])
        vec_rows = sb("vec_rows", [LAYERS * VECTORS, C])
        vec = sb("vec", [C, LAYERS * VECTORS])
        pw = sb("pw", [C, LAYERS, C])
        ones = sb("ones", [C, C])
        scale_diagonal = sb("scale_diagonal", [C, LAYERS, C])
        pw_bn = sb("pw_bn", [C + 1, LAYERS, C])
        wt = sb("wt", [C, SPLIT, TAPS, C])
        wt_high = sb("wt_high", [C, TAPS, C], F32R)
        wt_low = sb("wt_low", [C, TAPS, C], F32R)
        bn_scale = sb("bn_scale", [C, LAYERS])
        bn_bias = sb("bn_bias", [C, LAYERS])
        tmp = sb("tmp", [C, 8, LAYERS])
        zeros = sb("zeros", [C, W])
        x_in = sb("x_in", [Q, 2, CBLK, PX * C])
        ring = [sb(f"ring{l}", [C, RR * RW]) for l in range(SPLIT)]
        ring_high = sb("ring_high", [C, RR * RW], F32R)
        ring_low = sb("ring_low", [C, RR * RW], F32R)
        z = sb("z", [C + 1, SPLIT, 2, 2 * BLK])
        products = sb("products", [C, SPLIT, max(map(max, DMA_TAPS)), 2 * BLK])
        y = sb("y", [C, 2, 2 * BLK])
        y_out = sb("y_out", [Q, 2, CBLK, PX * C])

        conv_ps = [ps(f"conv_ps{i}", [C, 2, 512]) for i in range(2)]
        split_ps = ps("split_ps", [C, 2, 512])
        in_ps = ps("in_ps", [C, 512])
        out_ps = ps("out_ps", [Q, 512])

        vectors_loaded = sem("vectors_loaded")
        vectors_transposed = sem("vectors_transposed")
        setup = sem("setup")
        setup_sqrt = sem("setup_sqrt")
        dw_bias_product = sem("dw_bias_product")
        scale_ready = sem("scale_ready")
        scale_spread = sem("scale_spread")
        weights_ready = sem("weights_ready")
        rings_cleared = sem("rings_cleared")
        x_loaded = [sem(f"x_loaded{i}") for i in range(2)]
        x_transposed = sem("x_transposed")
        x_in_ring = sem("x_in_ring")
        conv_done = [sem(f"conv_done{l}") for l in range(LAYERS)]
        conv_out = [sem(f"conv_out{l}") for l in range(LAYERS)]
        low_ready = sem("low_ready")
        z_begun = [sem(f"z_begun{l}") for l in range(SPLIT)]
        z_summed = [sem(f"z_summed{l}") for l in range(SPLIT)]
        products_ready = [sem(f"products_ready{l}") for l in range(SPLIT)]
        products_summed = [sem(f"products_summed{l}") for l in range(SPLIT)]
        z_complete = [sem(f"z_complete{l}") for l in range(SPLIT)]
        adds_begun = sem("adds_begun")
        y_transposed = sem("y_transposed")
        y_ready = sem("y_ready")
        out_stored = [sem(f"out_stored{i}") for i in range(2)]

        ring_rows = [r[:, :].rearrange("c (r w) -> c r w", w=RW) for r in ring + [ring_high]]
        low_rows = ring_low[:, :].rearrange("c (r w) -> c r w", w=RW)

        def window(rows, pos, tap):
            dy, dx = tap // 3, tap % 3
            return rows[:, 4 * pos + dy:4 * pos + dy + ROWS_PAIR, dx:dx + W]

        def count(g, j, l, of):
            first = j - LAG * l
            each = [of((p + LAG * l) % 4, l) for p in range(4)]
            return sum(each) * (g + first // 4) + sum(each[:first % 4 + 1])

        def z_sums(g, j, l):
            return count(g, j, l, dve_taps)

        def product_sums(g, j, l):
            return count(g, j, l, lambda u, l: max(dma_taps(u, l) - 1, 0))

        def exists(g, p):
            return not isinstance(g, int) or 0 <= 4 * g + p < PAIRS

        def pairs_up_to(g, p):
            return min(4 * g + p + 1, PAIRS) if isinstance(g, int) else 4 * g + (p + 1)

        def positive(n):
            return not isinstance(n, int) or n > 0

        def load_parameters(queue, layers):
            for l in layers:
                v0 = l * VECTORS
                queue.dma_start(vec_rows[v0:v0 + TAPS, :],
                                params[l]["dw_kernel"].rearrange("a b i c -> (a b i) c")).then_inc(vectors_loaded, 16)
                for n, name in enumerate(VECTOR_NAMES):
                    queue.dma_start(vec_rows[v0 + TAPS + n:v0 + TAPS + n + 1, :],
                                    params[l][name].rearrange("(a c) -> a c", a=1)).then_inc(vectors_loaded, 16)
                queue.dma_start(pw[:, l, :],
                                params[l]["pw_kernel"].rearrange("a b c o -> (a b c) o")).then_inc(vectors_loaded, 16)

        block = ctx.enter_context(nc.Block())

        @block.sync
        def _(sp):
            def load(g, half):
                if not isinstance(g, int) or g > 0:
                    sp.wait_ge(x_transposed, 8 * g + 4 * half - 4)
                sp.dma_start(x_in[:, half, :, :], x_v[2 * g + half, :, :, :] if isinstance(g, int) else
                             x_v[bass.ds(2 * g + half, 1), :, :, :].rearrange("n q k f -> q (n k) f")
                             ).then_inc(x_loaded[half], 16)

            def store(n_half, half):
                sp.wait_ge(y_ready, 8 * n_half + 4 * half + 4)
                sp.dma_start(out_v[2 * n_half + half, :, :, :] if isinstance(n_half, int) else
                             out_v[bass.ds(2 * n_half + half, 1), :, :, :].rearrange("n q k f -> q (n k) f"),
                             y_out[:, half, :, :]).then_inc(out_stored[half], 16)

            load(0, 0)
            sp.dma_start(ident[:, :], identity_in).then_inc(vectors_loaded, 16)
            load_parameters(sp, range(LAYERS // 2))
            load(0, 1)
            for g in range(1, PEELED):
                for half in range(2):
                    load(g, half)
            with sp.Fori(PEELED, GROUPS) as g:
                load(g, 0)
                store(g - PEELED, 0)
                load(g, 1)
                store(g - PEELED, 1)
            for g in range(GROUPS - PEELED, GROUPS):
                store(g, 0)
                store(g, 1)
            for half in range(2):
                sp.wait_ge(out_stored[half], 16 * GROUPS)

        @block.gpsimd
        def _(pool):
            nc.gpsimd.memset(zeros[:, :], 0.0)
            nc.gpsimd.memset(ones[:, :], 1.0)
            nc.gpsimd.memset(z[C:C + 1, :, :, :], 1.0)
            for r in ring + [ring_high.bitcast(F32), ring_low.bitcast(F32)]:
                last = nc.gpsimd.memset(r[:, :], 0.0)
            last.then_inc(rings_cleared, 1)

            def add(into, addend):
                pool.sem_inc(adds_begun, 1)
                return pool.dma_start(into, addend, accum_op=ALU.add)

            def sum_products(g, j, l):
                if not exists(g, j - LAG * l):
                    return
                pool.wait_ge(products_ready[l], pairs_up_to(g, j - LAG * l))
                n = dma_taps(j % 4, l) - 1
                for k in range(n):
                    if k:
                        pool.wait_ge(products_summed[l], 16 * (product_sums(g, j, l) - n + k))
                    add(products[:, l, 0, :], products[:, l, 1 + k, :]).then_inc(products_summed[l], 16)

            def complete_z(g, j, l):
                p = j - LAG * l
                if not exists(g, p):
                    return
                pool.wait_ge(z_summed[l], z_sums(g, j, l))
                n = product_sums(g, j, l)
                if positive(n):
                    pool.wait_ge(products_summed[l], 16 * n)
                add(z[0:C, l, p % 2, :], products[:, l, 0, :]).then_inc(z_complete[l], 16)

            def group(g):
                for j in range(4):
                    sum_products(g, j + 1, 0)
                    complete_z(g, j, 2)
                    sum_products(g, j + 1, 1)
                    complete_z(g, j + 1, 0)
                    sum_products(g, j + 1, 2)
                    complete_z(g, j + 1, 1)

            sum_products(0, 0, 0)
            complete_z(0, 0, 0)
            for g in range(PEELED):
                group(g)
            with pool.Fori(PEELED, GROUPS - 1) as g:
                group(g)
            for g in range(GROUPS - 1, LAST_STEP // 4 + 1):
                group(g)

        @block.tensor
        def _(pe):
            pe.wait_ge(vectors_loaded, 16 * (1 + LAYERS * (2 + len(VECTOR_NAMES))))
            nv = LAYERS * VECTORS
            nc.tensor.transpose(in_ps[:, 0:nv], vec_rows[:, :], ident[0:nv, 0:nv]).then_inc(vectors_transposed, 1)
            pe.wait_ge(setup, 1)
            for l in range(LAYERS):
                last = nc.tensor.matmul(out_ps[0:C, l:l + 1], pw[:, l, :],
                                        vec[:, l * VECTORS + DW_BIAS:l * VECTORS + DW_BIAS + 1],
                                        start=True, stop=True)
            last.then_inc(dw_bias_product, 1)
            pe.wait_ge(rings_cleared, 1)
            pe.wait_ge(scale_ready, 1)
            for l in range(LAYERS):
                nc.tensor.matmul(conv_ps[0][:, 0, l * C:(l + 1) * C], ones[:, :], scale_diagonal[:, l, :],
                                 start=True, stop=True)
                last = nc.tensor.matmul(conv_ps[0][0:1, 1, l * C:(l + 1) * C], bn_bias[:, l:l + 1], ident[0:C, 0:C],
                                        start=True, stop=True)
            last.then_inc(scale_spread, 1)
            pe.wait_ge(weights_ready, 1)

            def transpose_in(g, j, b):
                if not exists(g, j):
                    return
                half = j % 4 // CHUNK
                if j % CHUNK == 0 and b == 0:
                    pe.wait_ge(x_loaded[half], 16 * (g + j // 4 + 1))
                before = 8 * g + 2 * j + b
                if positive(before):
                    pe.wait_ge(x_in_ring, before)
                for k in range(PX):
                    last = nc.tensor.transpose(in_ps[:, k * Q:(k + 1) * Q],
                                               x_in[:, half, 2 * (j % CHUNK) + b, k * C:(k + 1) * C],
                                               ident[0:Q, 0:Q])
                last.then_inc(x_transposed, 1)

            def transpose_out(g, j, b):
                if not exists(g, j):
                    return
                pe.wait_ge(conv_out[LAYERS - 1], pairs_up_to(g, j))
                before = 8 * g + 2 * j + b
                if positive(before):
                    pe.wait_ge(y_ready, before)
                pixels = y[:, j % 2, b * BLK:(b + 1) * BLK].rearrange("c (q k) -> c k q", k=PX)
                for k in range(PX):
                    last = nc.tensor.transpose(out_ps[:, k * C:(k + 1) * C], pixels[:, k, :], ident[0:C, 0:C])
                last.then_inc(y_transposed, 1)

            def conv(g, j, l):
                p = j - LAG * l
                if not exists(g, p):
                    return
                if l == 0:
                    pe.wait_ge(x_in_ring, 2 * pairs_up_to(g, p + 1))
                else:
                    pe.wait_ge(conv_out[l - 1], pairs_up_to(g, p + 1))
                step, k = (j, l - 2) if l >= 2 else (j - 1, l + SPLIT - 2)
                n = pairs_up_to(g, step - LAG * k)
                if positive(n):
                    pe.wait_ge(conv_out[k], n)
                    if k == SPLIT - 1:
                        pe.wait_ge(low_ready, n)
                taps = z_taps(j % 4, l)
                own = range(taps, TAPS)
                for i, tap in enumerate(own):
                    win = window(ring_rows[l], p % 4, tap)
                    for b in range(2):
                        last = nc.tensor.matmul(conv_ps[(j + l) % 2][:, b, 0:BLK], wt[:, l, tap, :],
                                                win[:, 2 * b:2 * b + 2, :], start=(i == 0), stop=False)
                pe.wait_ge(z_complete[l], 16 * pairs_up_to(g, p))
                for b in range(2):
                    last = nc.tensor.matmul(conv_ps[(j + l) % 2][:, b, 0:BLK], pw_bn[:, l, :],
                                            z[:, l, p % 2, b * BLK:(b + 1) * BLK],
                                            start=(len(own) == 0), stop=True)
                last.then_inc(conv_done[l], 1)

            def split_conv(g, j, dy):
                p = j - LAG * SPLIT
                if not exists(g, p):
                    return
                if dy == 0:
                    pe.wait_ge(conv_out[SPLIT - 1], pairs_up_to(g, p + 1))
                    pe.wait_ge(low_ready, pairs_up_to(g, p + 1))
                    n = pairs_up_to(g, p - 1)
                    if positive(n):
                        pe.wait_ge(conv_out[SPLIT], n)
                high_rows = ring_rows[SPLIT]
                passes = [(tap, weights, rows) for tap in range(3 * dy, 3 * dy + 3)
                          for weights, rows in ((wt_low, high_rows), (wt_high, low_rows), (wt_high, high_rows))]
                for i, (tap, weights, rows) in enumerate(passes):
                    win = window(rows, p % 4, tap)
                    for b in range(2):
                        last = nc.tensor.matmul(split_ps[:, b, 0:BLK], weights[:, tap, :], win[:, 2 * b:2 * b + 2, :],
                                                start=(dy == 0 and i == 0), stop=(dy == 2 and i == len(passes) - 1))
                if dy == 2:
                    last.then_inc(conv_done[SPLIT], 1)

            def group(g):
                for j in range(4):
                    conv(g, j, 0)
                    split_conv(g, j, 0)
                    transpose_out(g, j - OUT_LAG, 0)
                    transpose_in(g, j + X_LEAD, 0)
                    conv(g, j, 1)
                    split_conv(g, j, 1)
                    transpose_in(g, j + X_LEAD, 1)
                    conv(g, j, 2)
                    transpose_out(g, j - OUT_LAG, 1)
                    split_conv(g, j, 2)

            for j in range(X_LEAD):
                for b in range(2):
                    transpose_in(0, j, b)
            for g in range(PEELED):
                group(g)
            with pe.Fori(PEELED, GROUPS - 1) as g:
                group(g)
            for g in range(GROUPS - 1, LAST_STEP // 4 + 1):
                group(g)

        def inputs_in_ring(eng, g, j, l):
            p = j - LAG * l
            if l == 0:
                eng.wait_ge(x_in_ring, 2 * pairs_up_to(g, p + 1))
            else:
                eng.wait_ge(conv_out[l - 1], pairs_up_to(g, p + 1))

        def z_pair(l, p):
            return z[0:C, l, p % 2, :].rearrange("c (r w) -> c r w", w=W)

        @block.scalar
        def _(act):
            load_parameters(act, range(LAYERS // 2, LAYERS))
            act.wait_ge(setup, 2)
            nc.scalar.activation(tmp[:, 1, :], tmp[:, 0, :], ACT.Sqrt).then_inc(setup_sqrt, 1)
            act.wait_ge(rings_cleared, 1)
            act.wait_ge(weights_ready, 1)

            def last_pair(g, p):
                return isinstance(g, int) and 4 * g + p == PAIRS - 1

            def read_in(g, j, b, gm):
                if not exists(g, j):
                    return
                pos = j % 4
                image_group = None if gm is None else (gm + j // 4) % IMG
                n = pairs_up_to(g, j - 3)
                if b == 0 and positive(n):
                    act.wait_ge(conv_done[0], n)
                act.wait_ge(x_transposed, 8 * g + 2 * j + b + 1)
                rows = in_ps[:, 0:BLK].rearrange("c (k r q) -> c r q k", k=PX, r=2)
                if pos == 0 and b == 0:
                    dup = ring_rows[0][:, RR - 1, 1:W + 1]
                    if image_group == 0:
                        nc.scalar.activation(dup, zeros[:, :], ACT.Copy)
                    else:
                        nc.scalar.activation(dup.rearrange("c (q k) -> c q k", k=PX), rows[:, 0, :, :], ACT.Relu)
                if last_pair(g, j) and b == 1:
                    nc.scalar.activation(ring_rows[0][:, RR - 1, 1:W + 1], zeros[:, :], ACT.Copy)
                if pos == 3 and b == 1:
                    dup = ring_rows[0][:, 0, 1:W + 1]
                    if image_group == IMG - 1:
                        nc.scalar.activation(dup, zeros[:, :], ACT.Copy)
                    else:
                        nc.scalar.activation(dup.rearrange("c (q k) -> c q k", k=PX), rows[:, 1, :, :], ACT.Relu)
                r0 = 1 + 4 * pos + 2 * b
                nc.scalar.activation(ring_rows[0][:, r0:r0 + 2, 1:W + 1].rearrange("c r (q k) -> c r q k", k=PX),
                                     rows, ACT.Relu).then_inc(x_in_ring, 1)

            def read_conv(g, j, l, gm):
                p = j - LAG * l
                if not exists(g, p):
                    return
                act.wait_ge(conv_done[l], pairs_up_to(g, p))
                src = split_ps if l == SPLIT else conv_ps[(j + l) % 2]
                if l == LAYERS - 1:
                    n = 2 * pairs_up_to(g, p - 2)
                    if positive(n):
                        act.wait_ge(y_transposed, n)
                    nc.scalar.activation(y[:, p % 2, :].rearrange("c (b n) -> c b n", b=2), src[:, :, 0:BLK],
                                         ACT.Identity, bias=bn_bias[:, l:l + 1]).then_inc(conv_out[l], 1)
                    return
                n = pairs_up_to(g, p - 3)
                if positive(n):
                    act.wait_ge(conv_done[l + 1], n)
                pos = p % 4
                image_group = None if gm is None else (gm + p // 4) % IMG
                dst = ring_rows[l + 1]
                if pos == 0:
                    if image_group == 0:
                        nc.scalar.activation(dst[:, RR - 1, 1:W + 1], zeros[:, :], ACT.Copy)
                    else:
                        nc.scalar.activation(dst[:, RR - 1, 1:W + 1], src[:, 0, 0:W], ACT.Relu)
                if last_pair(g, p):
                    nc.scalar.activation(dst[:, RR - 1, 1:W + 1], zeros[:, :], ACT.Copy)
                if pos == 3:
                    if image_group == IMG - 1:
                        nc.scalar.activation(dst[:, 0, 1:W + 1], zeros[:, :], ACT.Copy)
                    else:
                        nc.scalar.activation(dst[:, 0, 1:W + 1], src[:, 1, W:BLK], ACT.Relu)
                r0 = 1 + 4 * pos
                nc.scalar.activation(dst[:, r0:r0 + 4, 1:W + 1].rearrange("c (b r) w -> c b r w", b=2),
                                     src[:, :, 0:BLK].rearrange("c b (r w) -> c b r w", w=W),
                                     ACT.Relu).then_inc(conv_out[l], 1)

            def begin_z(g, j, l):
                p = j - LAG * l
                if not exists(g, p):
                    return
                inputs_in_ring(act, g, j, l)
                n = pairs_up_to(g, p - 2)
                if positive(n):
                    act.wait_ge(conv_done[l], n)
                nc.scalar.activation(z_pair(l, p), window(ring_rows[l], p % 4, 0), ACT.Copy,
                                     scale=vec[:, l * VECTORS:l * VECTORS + 1]).then_inc(z_begun[l], 1)

            def write_products(g, j, l):
                p = j - LAG * l
                if not exists(g, p):
                    return
                before = pairs_up_to(g, p - 1)
                if positive(before):
                    act.wait_ge(z_complete[l], 16 * before)
                for k in range(dma_taps(j % 4, l)):
                    tap = l * VECTORS + 1 + k
                    last = nc.scalar.activation(products[:, l, k, :].rearrange("c (r w) -> c r w", w=W),
                                                window(ring_rows[l], p % 4, 1 + k), ACT.Copy, scale=vec[:, tap:tap + 1])
                last.then_inc(products_ready[l], 1)

            def read_out(g, j, b):
                if not exists(g, j):
                    return
                half = j % 4 // CHUNK
                if j % CHUNK == 0 and b == 0:
                    n = 16 * (g + j // 4)
                    if positive(n):
                        act.wait_ge(out_stored[half], n)
                act.wait_ge(y_transposed, 8 * g + 2 * j + b + 1)
                nc.scalar.activation(y_out[:, half, 2 * (j % CHUNK) + b, :], out_ps[:, 0:PX * C],
                                     ACT.Copy).then_inc(y_ready, 1)

            def group(g, gm):
                for j in range(4):
                    begin_z(g, j + 1, 0)
                    read_conv(g, j - 1, SPLIT, gm)
                    write_products(g, j + 1, 0)
                    read_conv(g, j, 0, gm)
                    begin_z(g, j + 1, 1)
                    write_products(g, j + 1, 1)
                    read_in(g, j + X_LEAD, 0, gm)
                    read_conv(g, j, 1, gm)
                    read_out(g, j - OUT_LAG, 0)
                    begin_z(g, j + 1, 2)
                    write_products(g, j + 1, 2)
                    read_conv(g, j, 2, gm)
                    read_out(g, j - OUT_LAG, 1)
                    read_in(g, j + X_LEAD, 1, gm)

            for j in range(X_LEAD):
                for b in range(2):
                    read_in(0, j, b, 0)
            begin_z(0, 0, 0)
            write_products(0, 0, 0)
            for g in range(PEELED):
                group(g, g)
            with act.Fori(0, B - 1) as image:
                with act.Fori(PEELED, IMG - 1) as k:
                    group(IMG * image + k, None)
                for k in range(IMG - 1, IMG + PEELED):
                    group(IMG * image + k, k % IMG)
            with act.Fori(IMG * (B - 1) + PEELED, GROUPS - 1) as g:
                group(g, None)
            for g in range(GROUPS - 1, LAST_STEP // 4 + 1):
                group(g, g % IMG)

        @block.vector
        def _(dve):
            done = [0]

            def link(instruction):
                done[0] += 1
                instruction.then_inc(setup, 1)
                dve.wait_ge(setup, done[0])

            col = lambda n: vec[:, n:n + VECTORS * (LAYERS - 1) + 1:VECTORS]
            dve.wait_ge(vectors_transposed, 1)
            link(nc.vector.tensor_copy(vec[:, :], in_ps[:, 0:LAYERS * VECTORS]))
            link(nc.vector.tensor_scalar_add(tmp[:, 0, :], col(VAR), BN_EPS))
            dve.wait_ge(setup_sqrt, 1)
            link(nc.vector.reciprocal(tmp[:, 2, :], tmp[:, 1, :]))
            link(nc.vector.tensor_tensor(tmp[:, 3, :], tmp[:, 0, :], tmp[:, 2, :], ALU.mult))
            link(nc.vector.tensor_tensor(tmp[:, 4, :], tmp[:, 1, :], tmp[:, 3, :], ALU.add))
            link(nc.vector.tensor_scalar(tmp[:, 5, :], tmp[:, 4, :], 0.5, None, ALU.mult))
            link(nc.vector.reciprocal(tmp[:, 6, :], tmp[:, 5, :]))
            link(nc.vector.tensor_tensor(bn_scale[:, :], col(GAMMA), tmp[:, 6, :], ALU.mult))
            dve.wait_ge(dw_bias_product, 1)
            link(nc.vector.tensor_tensor(tmp[:, 2, :], out_ps[0:C, 0:LAYERS], col(PW_BIAS), ALU.add))
            link(nc.vector.tensor_tensor(tmp[:, 3, :], tmp[:, 2, :], bn_scale[:, :], ALU.mult))
            link(nc.vector.tensor_tensor(tmp[:, 4, :], col(MEAN), bn_scale[:, :], ALU.mult))
            link(nc.vector.tensor_tensor(tmp[:, 5, :], col(BETA), tmp[:, 4, :], ALU.subtract))
            link(nc.vector.tensor_tensor(bn_bias[:, :], tmp[:, 3, :], tmp[:, 5, :], ALU.add))
            for l in range(LAYERS):
                last = nc.vector.tensor_scalar(scale_diagonal[:, l, :], ident[0:C, 0:C], bn_scale[:, l:l + 1], None,
                                               ALU.mult)
            last.then_inc(scale_ready, 1)
            dve.wait_ge(scale_spread, 1)
            nc.vector.tensor_copy(pw_bn[C:C + 1, :, :].rearrange("c l o -> c (l o)"), conv_ps[0][0:1, 1, 0:LAYERS * C])
            link(nc.vector.tensor_tensor(pw_bn[0:C, :, :].rearrange("c l o -> c (l o)"),
                                         pw[:, :, :].rearrange("c l o -> c (l o)"), conv_ps[0][:, 0, 0:LAYERS * C],
                                         ALU.mult))
            for l in range(SPLIT):
                for tap in range(TAPS):
                    n = l * VECTORS + tap
                    nc.vector.tensor_scalar(wt[:, l, tap, :], pw_bn[0:C, l, :], vec[:, n:n + 1], None, ALU.mult)
            for tap in range(TAPS):
                n = SPLIT * VECTORS + tap
                last = nc.vector.tensor_scalar(wt_high[:, tap, :], pw_bn[0:C, SPLIT, :], vec[:, n:n + 1], None,
                                               ALU.mult)
            link(last)
            for tap in range(TAPS):
                n = SPLIT * VECTORS + tap
                last = nc.vector.scalar_tensor_tensor(out=wt_low[:, tap, :], in0=pw_bn[0:C, SPLIT, :],
                                                      scalar=vec[:, n:n + 1], in1=wt_high[:, tap, :],
                                                      op0=ALU.mult, op1=ALU.subtract)
            last.then_inc(weights_ready, 1)

            def sum_taps(g, j, l, late):
                p = j - LAG * l
                if not exists(g, p):
                    return
                taps = range(1 + dma_taps(j % 4, l), z_taps(j % 4, l))
                before = z_sums(g, j, l) - len(taps)
                acc = z_pair(l, p)
                half = len(taps) // 2
                if not late:
                    dve.wait_ge(z_begun[l], pairs_up_to(g, p))
                for i in range(half, len(taps)) if late else range(half):
                    tap = taps[i]
                    weight = vec[:, l * VECTORS + tap:l * VECTORS + tap + 1]
                    if i:
                        dve.wait_ge(z_summed[l], before + i)
                    nc.vector.scalar_tensor_tensor(out=acc, in0=window(ring_rows[l], p % 4, tap), scalar=weight, in1=acc,
                                                   op0=ALU.mult, op1=ALU.add).then_inc(z_summed[l], 1)
                    yield

            def sum_z(g, j, l):
                turns = [sum_taps(g, j if l else j - 1, (l - 1) % SPLIT, True), sum_taps(g, j, l, False)]
                while turns:
                    turns = [t for t in turns if next(t, turns) is not turns]

            def low_part(g, j, gm):
                l = SPLIT - 1
                p = j - LAG * l
                if not exists(g, p):
                    return
                dve.wait_ge(conv_out[l], pairs_up_to(g, p))
                src = conv_ps[(j + l) % 2]
                high_rows = ring_rows[SPLIT]
                pos = p % 4
                image_group = None if gm is None else (gm + p // 4) % IMG

                def write_low(low, values, high):
                    return nc.vector.scalar_tensor_tensor(out=low, in0=values, scalar=0.0, in1=high,
                                                          op0=ALU.max, op1=ALU.subtract)

                if pos == 0:
                    if image_group == 0:
                        nc.vector.tensor_copy(low_rows[:, RR - 1, 1:W + 1], zeros[:, :])
                    else:
                        write_low(low_rows[:, RR - 1, 1:W + 1], src[:, 0, 0:W], high_rows[:, RR - 1, 1:W + 1])
                if isinstance(g, int) and 4 * g + p == PAIRS - 1:
                    nc.vector.tensor_copy(low_rows[:, RR - 1, 1:W + 1], zeros[:, :])
                if pos == 3:
                    if image_group == IMG - 1:
                        nc.vector.tensor_copy(low_rows[:, 0, 1:W + 1], zeros[:, :])
                    else:
                        write_low(low_rows[:, 0, 1:W + 1], src[:, 1, W:BLK], high_rows[:, 0, 1:W + 1])
                r0 = 1 + 4 * pos
                write_low(low_rows[:, r0:r0 + 4, 1:W + 1].rearrange("c (b r) w -> c b r w", b=2),
                          src[:, :, 0:BLK].rearrange("c b (r w) -> c b r w", w=W),
                          high_rows[:, r0:r0 + 4, 1:W + 1].rearrange("c (b r) w -> c b r w", b=2)
                          ).then_inc(low_ready, 1)

            def group(g, gm):
                for j in range(4):
                    sum_z(g, j + 1, 0)
                    sum_z(g, j + 1, 1)
                    sum_z(g, j + 1, 2)
                    low_part(g, j, gm)

            for l in range(SPLIT):
                sum_z(0, 0, l)
            for g in range(PEELED):
                group(g, g)
            with dve.Fori(0, B - 1) as image:
                with dve.Fori(PEELED, IMG - 1) as k:
                    group(IMG * image + k, None)
                for k in range(IMG - 1, IMG + PEELED):
                    group(IMG * image + k, k % IMG)
            with dve.Fori(IMG * (B - 1) + PEELED, GROUPS - 1) as g:
                group(g, None)
            for g in range(GROUPS - 1, LAST_STEP // 4 + 1):
                group(g, g % IMG)


_PER_LAYER = ["dw_kernel", "pw_kernel"] + VECTOR_NAMES


def kernel(**inputs):
    import numpy as _np
    import concourse.bacc as _bacc
    from concourse import mybir as _mybir
    from concourse.bass_utils import run_bass_kernel_spmd as _run

    nc = _bacc.Bacc("TRN2", target_bir_lowering=False, num_devices=1)
    arrays = {}

    def given(name, a):
        arrays[name] = a = _np.ascontiguousarray(a)
        return nc.dram_tensor(name, a.shape, _mybir.dt.from_np(a.dtype), kind="ExternalInput").ap()

    x = given("in_x_dram", inputs["x"])
    params = [{n: given(f"in_L{l}_{n}_dram", inputs[f"L{l}_conv_{n}"]) for n in _PER_LAYER} for l in range(LAYERS)]
    identity = given("in_identity_dram", _np.eye(128, dtype=_np.float32))
    out = nc.dram_tensor("out_0_dram", inputs["x"].shape, _mybir.dt.float32, kind="ExternalOutput").ap()
    conv_stack(nc, x, params, identity, out)
    r = _run(nc, [arrays], core_ids=[0])
    return r.results[0]["out_0_dram"]
```
